# Optimizing a Trainium2 kernel written in Bass

```python
import numpy as np
import jax
import jax.numpy as jnp

def _softmax(x, axis=-1):
    return jax.nn.softmax(x, axis=axis)

def _gelu(x):
    return jax.nn.gelu(x, approximate=True)

def _silu(x):
    return jax.nn.silu(x)

def _sigmoid(x):
    return jax.nn.sigmoid(x)

def _layernorm(x, axis=-1, eps=1e-05):
    m = jnp.mean(x, axis=axis, keepdims=True)
    v = jnp.var(x, axis=axis, keepdims=True)
    return (x - m) / jnp.sqrt(v + eps)

def _scatter_add(tgt, idx, src, axis=0):
    return tgt.at[idx].add(src)

def _segment_sum(src, seg, n):
    return jax.ops.segment_sum(src, seg, n)
kernel_name = 'mk_rec_standalone_d1_rec_r8_7edb0b'

def setup_inputs(seed: int=0):
    np.random.seed(seed)
    _w = jnp.asarray

    def _rec_inputs():
        import jax
        import jax.numpy as jnp
        _rk = jax.random.key(seed)
        r_x = -0.000520686 + 1.00062 * jax.random.normal(jax.random.fold_in(_rk, 1), (512, 2, 1024), jnp.float32)
        return r_x
    r_x = _rec_inputs()

    def _L0_rec_setup():
        import jax, jax.numpy as jnp
        import numpy as np
        B, L, D, F = (1024, 2, 1024, 4096)
        key = jax.random.key(seed)
        k1, k2, k3 = jax.random.split(key, 3)
        scale = 1.0 / np.sqrt(D)
        x = jax.random.normal(k1, (B, L, D), dtype=jnp.float32)
        W_enc = jax.random.normal(k2, (L, D, F), dtype=jnp.float32) * scale
        b_enc = jnp.zeros((F,), dtype=jnp.float32)
        W_dec = jax.random.normal(k3, (L, F, D), dtype=jnp.float32) * scale
        b_dec = jnp.zeros((L, D), dtype=jnp.float32)
        return {'x': x, 'W_enc': W_enc, 'b_enc': b_enc, 'W_dec': W_dec, 'b_dec': b_dec}
    _L0_rec_all = _L0_rec_setup()
    _L0_rec_in = {k: v for k, v in _L0_rec_all.items() if k in ('W_enc', 'b_enc', 'W_dec', 'b_dec')}
    del _L0_rec_all
    return {'r_x': r_x, 'L0_rec_W_enc': _L0_rec_in['W_enc'], 'L0_rec_b_enc': _L0_rec_in['b_enc'], 'L0_rec_W_dec': _L0_rec_in['W_dec'], 'L0_rec_b_dec': _L0_rec_in['b_dec']}

def reference(r_x, L0_rec_W_enc, L0_rec_b_enc, L0_rec_W_dec, L0_rec_b_dec):
    import jax
    import jax.numpy as jnp

    def _L0_rec_ref(x, W_enc, b_enc, W_dec, b_dec):
        import jax, jax.numpy as jnp
        import numpy as np
        B, L, D, F = (1024, 2, 1024, 4096)
        f = jax.nn.relu(jnp.einsum('bld,ldf->bf', x, W_enc) + b_enc)
        x_hat = jnp.einsum('bf,lfd->bld', f, W_dec) + b_dec
        return x_hat
    y = _L0_rec_ref(r_x, L0_rec_W_enc, L0_rec_b_enc, L0_rec_W_dec, L0_rec_b_dec)
    return y

_drawn_inputs = setup_inputs


def setup_inputs(seed=0):
    import zlib

    import numpy as np

    out = dict(_drawn_inputs(seed))
    spreads = {'L0_rec_b_enc': (0.0, 0.1), 'L0_rec_b_dec': (0.0, 0.1)}
    factors = {}
    for name, (base, spread) in spreads.items():
        noise = np.random.default_rng([zlib.crc32(name.encode()), seed]).standard_normal(out[name].shape)
        drawn = base * np.exp(spread * noise) if base else spread * noise
        out[name] = jnp.asarray(drawn.astype(out[name].dtype))
    for name, factor in factors.items():
        out[name] = (out[name] * factor).astype(out[name].dtype)
    return out
```

```python
from contextlib import ExitStack

import concourse.bass as bass
from concourse import mybir


def autoencoder_kernel(nc, xT, w_enc, b_enc, w_dec, b_dec, outT):
    F32 = mybir.dt.float32
    F32R = mybir.dt.float32r
    ACT = mybir.ActivationFunctionType
    ALU = mybir.AluOpType

    P = 128
    K, B = xT.shape
    LAYERS, F, D = w_dec.shape
    BANKS = 8
    W = BANKS * P
    ENC_K, DEC_K = K // P, F // P
    ENC_PASSES, DEC_PASSES = F // W, LAYERS * D // W
    assert D == W and B == 512

    SPLIT = 4
    RAW = 8
    AHEAD = SPLIT - 1
    assert ENC_K % RAW == 0 and DEC_K % RAW == 0 and RAW % SPLIT == 0
    PIECES = 4
    PIECE = W // PIECES
    WARM = 8
    ENC_ROUNDS, DEC_ROUNDS = ENC_K // RAW, DEC_K // RAW
    DEC_FIRST = ENC_PASSES * ENC_ROUNDS


    w_enc = w_enc.rearrange("l d f -> (l d) f")

    with ExitStack() as ctx:
        def sbuf(name, shape, dt=F32):
            return ctx.enter_context(nc.sbuf_tensor(name, shape, dt))

        def sem(name):
            return ctx.enter_context(nc.semaphore(name))

        x_sb = sbuf("x_sb", [P, ENC_K, B])
        f_sb = sbuf("f_sb", [P, DEC_K, B])
        w_raw = sbuf("w_raw", [P, RAW, W])
        w_hi = sbuf("w_hi", [P, SPLIT, W], F32R)
        w_lo = sbuf("w_lo", [P, SPLIT, W], F32R)
        v_hi = sbuf("v_hi", [P, SPLIT, B], F32R)
        v_lo = sbuf("v_lo", [P, SPLIT, B], F32R)
        out_sb = sbuf("out_sb", [P, BANKS, B])
        zeros = sbuf("zeros", [P, B], mybir.dt.bfloat16)
        b_enc_sb = sbuf("b_enc_sb", [P, DEC_K])
        b_dec_sb = sbuf("b_dec_sb", [P, DEC_PASSES * BANKS])
        sums = ctx.enter_context(nc.psum_tensor("sums", [P, BANKS, B], F32))

        w_loaded = [sem(f"w_loaded{s}") for s in range(RAW)]
        x_loaded = [sem(f"x_loaded{j}") for j in range(ENC_K)]
        bias_loaded = sem("bias_loaded")
        piece_loaded = [sem(f"piece_loaded{q}") for q in range(PIECES - 1)]
        hi_begun = sem("hi_begun")
        lo_begun = sem("lo_begun")
        zeros_set = sem("zeros_set")
        hi_done = sem("hi_done")
        lo_done = sem("lo_done")
        tile_multiplied = sem("tile_multiplied")
        bank_drained = sem("bank_drained")
        stored = [sem(f"stored{m}") for m in range(BANKS)]

        block = ctx.enter_context(nc.Block())

        @block.sync
        def _(sp):
            def load_w(src, rounds, j):
                if type(rounds) is not int or rounds * RAW + j >= RAW:
                    sp.wait_ge(lo_done, rounds * RAW + (j - RAW + 1))
                sp.dma_start(w_raw[:, j % RAW, :], src).then_inc(w_loaded[j % RAW], 16)

            def store(h):
                for m in range(BANKS):
                    sp.wait_ge(bank_drained, (ENC_PASSES + h) * BANKS + m + 1)
                    row = (h * BANKS + m) * P
                    sp.dma_start(outT[row:row + P, :], out_sb[:, m, :]).then_inc(stored[m], 16)

            for j in range(ENC_K):
                sp.dma_start(x_sb[:, j, :], xT[j * P:(j + 1) * P, :]).then_inc(x_loaded[j], 16)
                if j > 0:
                    load_w(w_enc[j * P:(j + 1) * P, 0:W], 0, j)
                else:
                    for q in range(PIECES):
                        cols = slice(q * PIECE, (q + 1) * PIECE)
                        sp.dma_start(w_raw[:, 0, cols], w_enc[0:P, cols]).then_inc(
                            piece_loaded[q] if q < PIECES - 1 else w_loaded[0], 16)
            sp.dma_start(b_enc_sb[:], b_enc).then_inc(bias_loaded, 16)
            sp.dma_start(b_dec_sb[:], b_dec).then_inc(bias_loaded, 16)
            with sp.Fori(1, ENC_PASSES) as g:
                for j in range(ENC_K):
                    load_w(w_enc[j * P:(j + 1) * P, bass.ds(g * W, W)], g * ENC_ROUNDS, j)
            for h in range(DEC_PASSES):
                first = DEC_FIRST + h * DEC_ROUNDS
                for j in range(RAW):
                    load_w(w_dec[h, j * P:(j + 1) * P, :], first, j)
                if h > 0:
                    store(h - 1)
                with sp.Fori(1, DEC_ROUNDS) as r:
                    for j in range(RAW):
                        load_w(w_dec[h, bass.ds(r * (RAW * P) + j * P, P), :], r + first, j)
            store(DEC_PASSES - 1)
            for m in range(BANKS):
                sp.wait_ge(stored[m], DEC_PASSES * 16)

        @block.scalar
        def _(act):
            def hi(v, rounds, j):
                act.wait_ge(w_loaded[j % RAW], (rounds + (j // RAW + 1)) * 16)
                if type(rounds) is not int or rounds * RAW + j >= SPLIT:
                    act.wait_ge(tile_multiplied, rounds * (RAW * BANKS) + (j + 1 - SPLIT) * BANKS)
                nc.scalar.copy(v_hi[:, j % SPLIT, :], v)
                nc.scalar.copy(w_hi[:, j % SPLIT, :], w_raw[:, j % RAW, :]).then_inc(hi_done, 1)

            def hi_x(rounds, j):
                act.wait_ge(x_loaded[j], 16)
                hi(x_sb[:, j, :], rounds, j)

            def drain_encoder(g, rounds):
                act.wait_ge(bias_loaded, 32)
                for m in range(BANKS):
                    act.wait_ge(tile_multiplied, rounds * (RAW * BANKS) + (m + 1 - BANKS))
                    tile = g * BANKS + m
                    nc.scalar.activation(f_sb[:, bass.ds(tile, 1), :], sums[:, m:m + 1, :], ACT.Relu,
                                         bias=b_enc_sb[:, bass.ds(tile, 1)]).then_inc(bank_drained, 1)

            def drain_decoder(h):
                rounds = DEC_FIRST + (h + 1) * DEC_ROUNDS
                for m in range(BANKS):
                    act.wait_ge(tile_multiplied, rounds * (RAW * BANKS) + (m + 1 - BANKS))
                    if h > 0:
                        act.wait_ge(stored[m], h * 16)
                    tile = h * BANKS + m
                    nc.scalar.activation(out_sb[:, m, :], sums[:, m, :], ACT.Identity,
                                         bias=b_dec_sb[:, tile:tile + 1]).then_inc(bank_drained, 1)

            act.wait_ge(x_loaded[0], 16)
            nc.scalar.copy(v_hi[:, 0, :], x_sb[:, 0, :]).then_inc(hi_begun, 1)
            for q in range(PIECES):
                cols = slice(q * PIECE, (q + 1) * PIECE)
                act.wait_ge(piece_loaded[q] if q < PIECES - 1 else w_loaded[0], 16)
                nc.scalar.copy(w_hi[:, 0, cols], w_raw[:, 0, cols]).then_inc(
                    hi_begun if q < PIECES - 1 else hi_done, 1)
            for j in range(1, SPLIT):
                hi_x(0, j)
            with act.Fori(0, ENC_PASSES - 1) as g:
                for j in range(SPLIT, ENC_K):
                    hi_x(g * ENC_ROUNDS, j)
                for j in range(AHEAD):
                    hi_x((g + 1) * ENC_ROUNDS, j)
                drain_encoder(g, (g + 1) * ENC_ROUNDS)
                hi_x((g + 1) * ENC_ROUNDS, AHEAD)
            for j in range(SPLIT, ENC_K):
                hi_x((ENC_PASSES - 1) * ENC_ROUNDS, j)
            act.wait_ge(bank_drained, (ENC_PASSES - 1) * BANKS)
            for j in range(AHEAD):
                hi(f_sb[:, j, :], DEC_FIRST, j)
            drain_encoder(ENC_PASSES - 1, DEC_FIRST)
            act.wait_ge(bank_drained, ENC_PASSES * BANKS)
            for h in range(DEC_PASSES):
                first = DEC_FIRST + h * DEC_ROUNDS
                for j in range(AHEAD, RAW):
                    hi(f_sb[:, j, :], first, j)
                with act.Fori(1, DEC_ROUNDS) as r:
                    for j in range(RAW):
                        hi(f_sb[:, bass.ds(r * RAW + j, 1), :], r + first, j)
                if h + 1 < DEC_PASSES:
                    for j in range(AHEAD):
                        hi(f_sb[:, j, :], first + DEC_ROUNDS, j)
                drain_decoder(h)

        @block.vector
        def _(dve):
            def lo(v, rounds, j):
                dve.wait_ge(hi_done, rounds * RAW + (j + 1))
                nc.vector.tensor_tensor(v_lo[:, j % SPLIT, :], v, v_hi[:, j % SPLIT, :].bitcast(F32),
                                        ALU.subtract)
                nc.vector.tensor_tensor(w_lo[:, j % SPLIT, :], w_raw[:, j % RAW, :],
                                        w_hi[:, j % SPLIT, :].bitcast(F32),
                                        ALU.subtract).then_inc(lo_done, 1)

            nc.vector.memset(zeros[:], 0.0).then_inc(zeros_set, 1)
            dve.wait_ge(hi_begun, 1)
            nc.vector.tensor_tensor(v_lo[:, 0, :], x_sb[:, 0, :], v_hi[:, 0, :].bitcast(F32),
                                    ALU.subtract).then_inc(lo_begun, 1)
            for q in range(PIECES):
                cols = slice(q * PIECE, (q + 1) * PIECE)
                if q < PIECES - 1:
                    dve.wait_ge(hi_begun, q + 2)
                else:
                    dve.wait_ge(hi_done, 1)
                nc.vector.tensor_tensor(w_lo[:, 0, cols], w_raw[:, 0, cols], w_hi[:, 0, cols].bitcast(F32),
                                        ALU.subtract).then_inc(lo_begun if q < PIECES - 1 else lo_done, 1)
            for j in range(1, ENC_K):
                lo(x_sb[:, j, :], 0, j)
            with dve.Fori(1, ENC_PASSES) as g:
                for j in range(ENC_K):
                    lo(x_sb[:, j, :], g * ENC_ROUNDS, j)
            for h in range(DEC_PASSES):
                first = DEC_FIRST + h * DEC_ROUNDS
                with dve.Fori(0, DEC_ROUNDS) as r:
                    for j in range(RAW):
                        lo(f_sb[:, bass.ds(r * RAW + j, 1), :], r + first, j)

        @block.tensor
        def _(pe):
            def multiply(rounds, j, start=False, stop=False, drained=None):
                pe.wait_ge(hi_done, rounds * RAW + (j + 1))
                pe.wait_ge(lo_done, rounds * RAW + (j + 1))
                s = j % SPLIT
                for m in range(BANKS):
                    if drained is not None:
                        pe.wait_ge(bank_drained, drained + (m + 1))
                    cols = slice(m * P, (m + 1) * P)
                    out = sums[:, m, :]
                    nc.tensor.matmul(out, w_hi[:, s, cols], v_hi[:, s, :], start=start, stop=False)
                    nc.tensor.matmul(out, w_hi[:, s, cols], v_lo[:, s, :], start=False, stop=False)
                    nc.tensor.matmul(out, w_lo[:, s, cols], v_hi[:, s, :], start=False,
                                     stop=stop).then_inc(tile_multiplied, 1)

            pe.wait_ge(zeros_set, 1)
            for _ in range(WARM):
                nc.tensor.matmul(sums[:, BANKS - 1, :], zeros[:, 0:P], zeros[:], start=True, stop=True)
            for m in range(BANKS):
                q = m * P // PIECE
                if q < PIECES - 1:
                    pe.wait_ge(hi_begun, q + 2)
                else:
                    pe.wait_ge(hi_done, 1)
                cols = slice(m * P, (m + 1) * P)
                out = sums[:, m, :]
                nc.tensor.matmul(out, w_hi[:, 0, cols], v_hi[:, 0, :], start=True, stop=False)
                if m == 0:
                    pe.wait_ge(lo_begun, 1)
                nc.tensor.matmul(out, w_hi[:, 0, cols], v_lo[:, 0, :], start=False, stop=False)
                if q < PIECES - 1:
                    pe.wait_ge(lo_begun, q + 2)
                else:
                    pe.wait_ge(lo_done, 1)
                nc.tensor.matmul(out, w_lo[:, 0, cols], v_hi[:, 0, :], start=False,
                                 stop=False).then_inc(tile_multiplied, 1)
            with pe.Fori(0, ENC_PASSES) as g:
                for j in range(1, ENC_K):
                    multiply(g * ENC_ROUNDS, j, stop=j == ENC_K - 1)
                multiply((g + 1) * ENC_ROUNDS, 0, start=True, drained=g * BANKS)
            for h in range(DEC_PASSES):
                first = DEC_FIRST + h * DEC_ROUNDS
                if h > 0:
                    multiply(first, 0, start=True, drained=(ENC_PASSES + h - 1) * BANKS)
                for j in range(1, RAW):
                    multiply(first, j)
                with pe.Fori(1, DEC_ROUNDS - 1) as r:
                    for j in range(RAW):
                        multiply(r + first, j)
                for j in range(RAW):
                    multiply(first + DEC_ROUNDS - 1, j, stop=j == RAW - 1)


def kernel(r_x, L0_rec_W_enc, L0_rec_b_enc, L0_rec_W_dec, L0_rec_b_dec):
    import numpy as np
    import concourse.bacc as bacc
    from concourse.bass_utils import run_bass_kernel_spmd

    x, w_enc, b_enc, w_dec, b_dec = (np.asarray(a) for a in (
        r_x, L0_rec_W_enc, L0_rec_b_enc, L0_rec_W_dec, L0_rec_b_dec))
    batch, layers, width = x.shape
    arrays = {
        "xT": np.ascontiguousarray(x.reshape(batch, layers * width).T),
        "w_enc": np.ascontiguousarray(w_enc),
        "b_enc": np.ascontiguousarray(b_enc.reshape(-1, 128).T),
        "w_dec": np.ascontiguousarray(w_dec),
        "b_dec": np.ascontiguousarray(b_dec.reshape(-1, 128).T),
    }
    nc = bacc.Bacc("TRN2", target_bir_lowering=False, num_devices=1)
    args = [nc.dram_tensor(name, a.shape, mybir.dt.from_np(a.dtype), kind="ExternalInput").ap()
            for name, a in arrays.items()]
    out = nc.dram_tensor("outT", (layers * width, batch), mybir.dt.float32, kind="ExternalOutput").ap()
    autoencoder_kernel(nc, *args, out)
    result = run_bass_kernel_spmd(nc, [arrays], core_ids=[0])
    outT = result.results[0]["outT"]
    return np.ascontiguousarray(outT.T).reshape(batch, layers, width)
```
